# Optimizing a Trainium2 kernel written in Bass

```python
import numpy as np
import jax
import jax.numpy as jnp

def _softmax(x, axis=-1):
    return jax.nn.softmax(x, axis=axis)

def _gelu(x):
    return jax.nn.gelu(x, approximate=True)

def _silu(x):
    return jax.nn.silu(x)

def _sigmoid(x):
    return jax.nn.sigmoid(x)

def _layernorm(x, axis=-1, eps=1e-05):
    m = jnp.mean(x, axis=axis, keepdims=True)
    v = jnp.var(x, axis=axis, keepdims=True)
    return (x - m) / jnp.sqrt(v + eps)

def _scatter_add(tgt, idx, src, axis=0):
    return tgt.at[idx].add(src)

def _segment_sum(src, seg, n):
    return jax.ops.segment_sum(src, seg, n)
kernel_name = 'mk_dlrm_tower_d1_rec_r8_80fd6e'

def setup_inputs(seed: int=0):
    np.random.seed(seed)
    _w = jnp.asarray

    def _rec_inputs():
        import jax
        import jax.numpy as jnp
        _tk = jax.random.key(seed)
        dense_ctx = jax.random.normal(jax.random.fold_in(_tk, 190), (2048, 16), jnp.float32)
        ids = jnp.stack([jax.random.randint(jax.random.fold_in(_tk, 200 + f), (2048,), 0, v, jnp.int32) for f, v in enumerate([12500, 1250, 12500, 12500, 1250, 1000, 1000, 125000, 1000, 1000, 1000, 1000, 1000, 1250, 1000, 1000, 12500, 1000, 1250, 1000, 1250, 1000, 12500, 12500, 1000, 12500, 1000])], axis=1)
        tbl_0 = 0.05 * jax.random.normal(jax.random.fold_in(_tk, 500 + 0), (12500, 128), jnp.float32)
        tbl_1 = 0.05 * jax.random.normal(jax.random.fold_in(_tk, 500 + 1), (1250, 128), jnp.float32)
        tbl_2 = 0.05 * jax.random.normal(jax.random.fold_in(_tk, 500 + 2), (12500, 128), jnp.float32)
        tbl_3 = 0.05 * jax.random.normal(jax.random.fold_in(_tk, 500 + 3), (12500, 128), jnp.float32)
        tbl_4 = 0.05 * jax.random.normal(jax.random.fold_in(_tk, 500 + 4), (1250, 128), jnp.float32)
        tbl_5 = 0.05 * jax.random.normal(jax.random.fold_in(_tk, 500 + 5), (1000, 128), jnp.float32)
        tbl_6 = 0.05 * jax.random.normal(jax.random.fold_in(_tk, 500 + 6), (1000, 128), jnp.float32)
        tbl_7 = 0.05 * jax.random.normal(jax.random.fold_in(_tk, 500 + 7), (125000, 128), jnp.float32)
        tbl_8 = 0.05 * jax.random.normal(jax.random.fold_in(_tk, 500 + 8), (1000, 128), jnp.float32)
        tbl_9 = 0.05 * jax.random.normal(jax.random.fold_in(_tk, 500 + 9), (1000, 128), jnp.float32)
        tbl_10 = 0.05 * jax.random.normal(jax.random.fold_in(_tk, 500 + 10), (1000, 128), jnp.float32)
        tbl_11 = 0.05 * jax.random.normal(jax.random.fold_in(_tk, 500 + 11), (1000, 128), jnp.float32)
        tbl_12 = 0.05 * jax.random.normal(jax.random.fold_in(_tk, 500 + 12), (1000, 128), jnp.float32)
        tbl_13 = 0.05 * jax.random.normal(jax.random.fold_in(_tk, 500 + 13), (1250, 128), jnp.float32)
        tbl_14 = 0.05 * jax.random.normal(jax.random.fold_in(_tk, 500 + 14), (1000, 128), jnp.float32)
        tbl_15 = 0.05 * jax.random.normal(jax.random.fold_in(_tk, 500 + 15), (1000, 128), jnp.float32)
        tbl_16 = 0.05 * jax.random.normal(jax.random.fold_in(_tk, 500 + 16), (12500, 128), jnp.float32)
        tbl_17 = 0.05 * jax.random.normal(jax.random.fold_in(_tk, 500 + 17), (1000, 128), jnp.float32)
        tbl_18 = 0.05 * jax.random.normal(jax.random.fold_in(_tk, 500 + 18), (1250, 128), jnp.float32)
        tbl_19 = 0.05 * jax.random.normal(jax.random.fold_in(_tk, 500 + 19), (1000, 128), jnp.float32)
        tbl_20 = 0.05 * jax.random.normal(jax.random.fold_in(_tk, 500 + 20), (1250, 128), jnp.float32)
        tbl_21 = 0.05 * jax.random.normal(jax.random.fold_in(_tk, 500 + 21), (1000, 128), jnp.float32)
        tbl_22 = 0.05 * jax.random.normal(jax.random.fold_in(_tk, 500 + 22), (12500, 128), jnp.float32)
        tbl_23 = 0.05 * jax.random.normal(jax.random.fold_in(_tk, 500 + 23), (12500, 128), jnp.float32)
        tbl_24 = 0.05 * jax.random.normal(jax.random.fold_in(_tk, 500 + 24), (1000, 128), jnp.float32)
        tbl_25 = 0.05 * jax.random.normal(jax.random.fold_in(_tk, 500 + 25), (12500, 128), jnp.float32)
        tbl_26 = 0.05 * jax.random.normal(jax.random.fold_in(_tk, 500 + 26), (1000, 128), jnp.float32)
        _rk = jax.random.fold_in(_tk, 7)
        W_top1 = 0.0161733 * jax.random.normal(jax.random.fold_in(_tk, 801), (3823, 512), jnp.float32)
        W_top2 = 0.0441942 * jax.random.normal(jax.random.fold_in(_tk, 802), (512, 256), jnp.float32)
        W_top3 = 0.0625 * jax.random.normal(jax.random.fold_in(_tk, 803), (256, 1), jnp.float32)
        b_top1 = jnp.zeros((512,), jnp.float32)
        b_top2 = jnp.zeros((256,), jnp.float32)
        return (dense_ctx, ids, tbl_0, tbl_1, tbl_2, tbl_3, tbl_4, tbl_5, tbl_6, tbl_7, tbl_8, tbl_9, tbl_10, tbl_11, tbl_12, tbl_13, tbl_14, tbl_15, tbl_16, tbl_17, tbl_18, tbl_19, tbl_20, tbl_21, tbl_22, tbl_23, tbl_24, tbl_25, tbl_26, W_top1, b_top1, W_top2, b_top2, W_top3)
    dense_ctx, ids, tbl_0, tbl_1, tbl_2, tbl_3, tbl_4, tbl_5, tbl_6, tbl_7, tbl_8, tbl_9, tbl_10, tbl_11, tbl_12, tbl_13, tbl_14, tbl_15, tbl_16, tbl_17, tbl_18, tbl_19, tbl_20, tbl_21, tbl_22, tbl_23, tbl_24, tbl_25, tbl_26, W_top1, b_top1, W_top2, b_top2, W_top3 = _rec_inputs()

    def _L0_rec_setup():
        import jax, jax.numpy as jnp
        import numpy as np
        NUM_FEATURES = 27
        FEATURE_DIM = 128
        BATCH = 2048
        _TRIU_I, _TRIU_J = np.triu_indices(NUM_FEATURES, k=1)
        key = jax.random.key(seed)
        embeddings = jax.random.normal(key, (BATCH, NUM_FEATURES, FEATURE_DIM), dtype=jnp.float32)
        return {'embeddings': embeddings}
    _L0_rec_all = _L0_rec_setup()
    _L0_rec_in = {k: v for k, v in _L0_rec_all.items() if k in ()}
    del _L0_rec_all
    return {'dense_ctx': dense_ctx, 'ids': ids, 'tbl_0': tbl_0, 'tbl_1': tbl_1, 'tbl_2': tbl_2, 'tbl_3': tbl_3, 'tbl_4': tbl_4, 'tbl_5': tbl_5, 'tbl_6': tbl_6, 'tbl_7': tbl_7, 'tbl_8': tbl_8, 'tbl_9': tbl_9, 'tbl_10': tbl_10, 'tbl_11': tbl_11, 'tbl_12': tbl_12, 'tbl_13': tbl_13, 'tbl_14': tbl_14, 'tbl_15': tbl_15, 'tbl_16': tbl_16, 'tbl_17': tbl_17, 'tbl_18': tbl_18, 'tbl_19': tbl_19, 'tbl_20': tbl_20, 'tbl_21': tbl_21, 'tbl_22': tbl_22, 'tbl_23': tbl_23, 'tbl_24': tbl_24, 'tbl_25': tbl_25, 'tbl_26': tbl_26, 'W_top1': W_top1, 'b_top1': b_top1, 'W_top2': W_top2, 'b_top2': b_top2, 'W_top3': W_top3}

def reference(dense_ctx, ids, tbl_0, tbl_1, tbl_2, tbl_3, tbl_4, tbl_5, tbl_6, tbl_7, tbl_8, tbl_9, tbl_10, tbl_11, tbl_12, tbl_13, tbl_14, tbl_15, tbl_16, tbl_17, tbl_18, tbl_19, tbl_20, tbl_21, tbl_22, tbl_23, tbl_24, tbl_25, tbl_26, W_top1, b_top1, W_top2, b_top2, W_top3):
    import jax
    import jax.numpy as jnp

    def _L0_rec_ref(embeddings):
        import jax, jax.numpy as jnp
        import numpy as np
        NUM_FEATURES = 27
        FEATURE_DIM = 128
        BATCH = 2048
        _TRIU_I, _TRIU_J = np.triu_indices(NUM_FEATURES, k=1)
        B = embeddings.shape[0]
        interactions = jnp.einsum('bfd,bgd->bfg', embeddings, embeddings)
        flat_interactions = interactions[:, _TRIU_I, _TRIU_J]
        flat_embeddings = embeddings.reshape(B, -1)
        return jnp.concatenate([flat_embeddings, flat_interactions], axis=1)
    e = jnp.stack([tbl_0[ids[:, 0]], tbl_1[ids[:, 1]], tbl_2[ids[:, 2]], tbl_3[ids[:, 3]], tbl_4[ids[:, 4]], tbl_5[ids[:, 5]], tbl_6[ids[:, 6]], tbl_7[ids[:, 7]], tbl_8[ids[:, 8]], tbl_9[ids[:, 9]], tbl_10[ids[:, 10]], tbl_11[ids[:, 11]], tbl_12[ids[:, 12]], tbl_13[ids[:, 13]], tbl_14[ids[:, 14]], tbl_15[ids[:, 15]], tbl_16[ids[:, 16]], tbl_17[ids[:, 17]], tbl_18[ids[:, 18]], tbl_19[ids[:, 19]], tbl_20[ids[:, 20]], tbl_21[ids[:, 21]], tbl_22[ids[:, 22]], tbl_23[ids[:, 23]], tbl_24[ids[:, 24]], tbl_25[ids[:, 25]], tbl_26[ids[:, 26]]], axis=1)
    z = _L0_rec_ref(e)
    z = z.reshape(z.shape[0], -1)
    h = jnp.concatenate([z, dense_ctx], axis=1)
    h = jnp.maximum(h @ W_top1 + b_top1, 0.0)
    h = jnp.maximum(h @ W_top2 + b_top2, 0.0)
    y = h @ W_top3
    return y

_drawn_inputs = setup_inputs


def setup_inputs(seed=0):
    import zlib

    import numpy as np

    out = dict(_drawn_inputs(seed))
    spreads = {'b_top1': (0.0, 0.1), 'b_top2': (0.0, 0.1)}
    factors = {}
    for name, (base, spread) in spreads.items():
        noise = np.random.default_rng([zlib.crc32(name.encode()), seed]).standard_normal(out[name].shape)
        drawn = base * np.exp(spread * noise) if base else spread * noise
        out[name] = jnp.asarray(drawn.astype(out[name].dtype))
    for name, factor in factors.items():
        out[name] = (out[name] * factor).astype(out[name].dtype)
    return out
```

```python
from contextlib import ExitStack

import concourse.bass as bass
from concourse import mybir

F32 = mybir.dt.float32
F32R = mybir.dt.float32r
I32 = mybir.dt.int32
ACT = mybir.ActivationFunctionType
ALU = mybir.AluOpType

P = 128


def pair_layout(features, ctx_rows):
    deltas = (features - 1) // 2
    per_chunk = features // 3
    first_pair = features * P
    first_ctx = first_pair + features * (features - 1) // 2
    room = P - per_chunk * deltas
    ctx_in_chunk = [min(room, ctx_rows), ctx_rows - min(room, ctx_rows), 0]
    rows, taken = [], 0
    for c in range(3):
        rows.append([first_ctx + taken + k for k in range(ctx_in_chunk[c])])
        taken += ctx_in_chunk[c]
        for i in range(c * per_chunk, (c + 1) * per_chunk):
            for delta in range(1, deltas + 1):
                a, b = sorted((i, (i + delta) % features))
                rows[c].append(first_pair + a * features - a * (a + 1) // 2 + b - a - 1)
    return rows, ctx_in_chunk


def dlrm_tower(nc, ids, tables, ctx_t, w_dense, w_pairs, b1_t, w2, b2, w3, eye, out):
    B, NF = ids.shape
    D = tables[0].shape[1]
    HID1 = w_dense.shape[1]
    HID2 = w2.shape[1]
    TILES = B // P
    CTX = ctx_t.shape[0]
    assert D == P and B % P == 0 and TILES % 2 == 0 and NF % 3 == 0 and NF % 2 == 1
    assert HID1 == 512 and HID2 <= 512 and HID1 % P == 0

    pair_rows, ctx_in_chunk = pair_layout(NF, CTX)
    DELTAS = (NF - 1) // 2
    ROWS_I = NF // 3
    K_PAIR = [len(r) for r in pair_rows]
    CHUNKS = NF + 3
    C1 = HID1 // P

    QUADS = [list(range(f, min(f + 4, NF))) for f in range(0, NF, 4)]
    NQ = len(QUADS)
    SLOTS = 32
    GROUPS = P // 2
    COLS = NF + 1
    BATCH_G = 8
    NB = GROUPS // BATCH_G
    WRAP = DELTAS
    WIDE = NF + WRAP
    STAGES = 4

    ids_t = ids.rearrange("(t p) f -> t p f", p=P)
    out_t = out.rearrange("(t p) o -> t p o", p=P)

    same_d = nc.dram_tensor("pairs_same_dram", [2, SLOTS, WIDE, GROUPS], F32, kind="Internal")
    cross_d = nc.dram_tensor("pairs_cross_dram", [2, WIDE, NF, GROUPS], F32, kind="Internal")
    same_ap, cross_ap = same_d.ap(), cross_d.ap()

    with ExitStack() as ctx:
        def sb(name, shape, dt=F32):
            return ctx.enter_context(nc.sbuf_tensor(name, shape, dt))

        def pb(name, shape):
            return ctx.enter_context(nc.psum_tensor(name, shape, F32))

        def sem(name):
            return ctx.enter_context(nc.semaphore(name))

        w1_high = sb("w1_high", [P, CHUNKS, HID1], F32R)
        w1_low = sb("w1_low", [P, CHUNKS, HID1], F32R)
        w2_high = sb("w2_high", [P, C1, HID2], F32R)
        w2_low = sb("w2_low", [P, C1, HID2], F32R)
        b1_sb = sb("b1_sb", [P, C1])
        b2_rows = sb("b2_rows", [P, HID2])
        w3_rows = sb("w3_rows", [P, HID2])
        identity = sb("identity", [P, P])
        w_stage = sb("w_stage", [P, STAGES, HID1])
        idx = sb("idx", [P, 2, NF], I32)
        gathered = sb("gathered", [P, NF, D])
        emb = sb("emb", [P, P, 2, SLOTS], F32R)
        emb_f32 = emb[:].bitcast(F32)
        prod = sb("prod", [P, NF, GROUPS])
        inter = sb("inter", [P, 3, P])
        inter_cross = sb("inter_cross", [P, 3, P])
        inter_high = sb("inter_high", [P, 3, P], F32R)
        inter_low = sb("inter_low", [P, 3, P], F32R)
        inter_high_f32 = inter_high[:].bitcast(F32)
        hid1 = sb("hid1", [P, HID1])
        hid1_relu = sb("hid1_relu", [P, C1, P])
        hid1_high = sb("hid1_high", [P, C1, P], F32R)
        hid1_low = sb("hid1_low", [P, C1, P], F32R)
        hid1_high_f32 = hid1_high[:].bitcast(F32)
        hid2 = sb("hid2", [P, HID2])
        y = sb("y", [P, 2, 1])

        p_hid1 = [pb(f"p_hid1_{k}", [P, HID1]) for k in range(2)]
        p_quad = [pb(f"p_quad_{k}", [P, 4, P]) for k in range(2)]
        p_prod = [pb(f"p_prod_{k}", [P, 512]) for k in range(2)]
        p_hid1_t = pb("p_hid1_t", [P, C1, P])
        p_hid2 = pb("p_hid2", [P, 512])

        consts_loaded = sem("consts_loaded")
        w_loaded = [sem(f"w_loaded_{k}") for k in range(STAGES)]
        ids_loaded = [sem(f"ids_loaded_{k}") for k in range(2)]
        quad_gathered = [sem(f"quad_gathered_{q}") for q in range(NQ)]
        prod_stored = sem("prod_stored")
        pairs_loaded = sem("pairs_loaded")
        y_stored = sem("y_stored")
        quads_free = sem("quads_free")
        steps_reached = sem("steps_reached")
        quad_transposed = sem("quad_transposed")
        prod_batch_done = sem("prod_batch_done")
        hid1_done = sem("hid1_done")
        hid1_transposed = sem("hid1_transposed")
        hid2_done = sem("hid2_done")
        w_high_done = sem("w_high_done")
        quad_high_done = sem("quad_high_done")
        low_rows_copied = sem("low_rows_copied")
        inter_high_done = sem("inter_high_done")
        hid1_relu_done = sem("hid1_relu_done")
        hid1_high_done = sem("hid1_high_done")
        zeroed = sem("zeroed")
        w_low_done = sem("w_low_done")
        quad_low_done = sem("quad_low_done")
        prod_summed = sem("prod_summed")
        inter_summed = sem("inter_summed")
        inter_low_done = sem("inter_low_done")
        hid1_copied = sem("hid1_copied")
        hid1_low_done = sem("hid1_low_done")
        hid2_step = sem("hid2_step")
        y_ready = sem("y_ready")

        def wait(eng, s, value, carrier=None):
            if not isinstance(value, int) or value > 0:
                eng.wait_ge(s, value)
                if carrier is not None and not isinstance(value, int):
                    eng.sem_inc(carrier, 1)

        def by_group(x):
            return x.rearrange("p c (s g) -> p c s g", s=2)

        def by_half(x):
            return x.rearrange("p c (g s) -> p c s g", s=2)

        W1_CHUNKS = [("w1", c, P if c < NF else K_PAIR[c - NF]) for c in range(CHUNKS)]
        W2_PAIRS = [("w2", c, P) for c in range(0, C1, 2)]
        STAGED = W1_CHUNKS + W2_PAIRS
        pair_base = [sum(K_PAIR[:c]) for c in range(3)]
        PAIR_DMAS = 2 * 3 * 2 + sum(1 for n in ctx_in_chunk if n)
        STORES = 6
        CONSTS = 4

        block = ctx.enter_context(nc.Block())

        @block.sync
        def _(sp):
            def load_ids(t, par):
                sp.dma_start(idx[:, par, :], ids_t[t]).then_inc(ids_loaded[par], 16)

            def load_weight(n):
                kind, c, rows = STAGED[n]
                wait(sp, w_low_done, n - STAGES + 1, steps_reached)
                slot = n % STAGES
                if kind == "w1" and c < NF:
                    src, dst = w_dense[c * P:(c + 1) * P, :], w_stage[:, slot, :]
                elif kind == "w1":
                    src = w_pairs[pair_base[c - NF]:pair_base[c - NF] + rows, :]
                    dst = w_stage[0:rows, slot, :]
                else:
                    src = w2.rearrange("(c p) n -> p c n", p=P)[:, c:c + 2, :]
                    dst = w_stage[:, slot, :].rearrange("p (c n) -> p c n", c=2)
                sp.dma_start(dst, src).then_inc(w_loaded[slot], 16)

            def pairs_round_trip(t):
                wait(sp, prod_summed, (t + 1) * NB, steps_reached)
                wait(sp, pairs_loaded, t * (PAIR_DMAS * 16), steps_reached)
                sp.dma_start(same_ap.rearrange("s r c g -> (s r) c g")[:, 0:NF, :],
                             prod[0:64, :, :]).then_inc(prod_stored, 16)
                sp.dma_start(same_ap.rearrange("s r c g -> (s r) c g")[:, NF:WIDE, :],
                             prod[0:64, 0:WRAP, :]).then_inc(prod_stored, 16)
                for s in range(2):
                    lo = 64 + SLOTS * s
                    sp.dma_start(cross_ap[s, 0:NF], prod[lo:lo + NF, :, :]).then_inc(prod_stored, 16)
                    sp.dma_start(cross_ap[s, NF:WIDE],
                                 prod[lo:lo + WRAP, :, :]).then_inc(prod_stored, 16)
                wait(sp, inter_high_done, t, steps_reached)
                wait(sp, inter_low_done, t, steps_reached)
                k = 0
                for c in range(3):
                    n = ctx_in_chunk[c]
                    if n:
                        sp.dma_start(inter[0:n, c, :],
                                     ctx_t[k:k + n, bass.ds(t * P, P)]).then_inc(pairs_loaded, 16)
                        k += n
                wait(sp, prod_stored, (t + 1) * (STORES * 16), steps_reached)
                for c in range(3):
                    lo = ctx_in_chunk[c]
                    for s in range(2):
                        i0 = c * ROWS_I
                        dst = (slice(lo, lo + ROWS_I * DELTAS), c, slice(GROUPS * s, GROUPS * (s + 1)))
                        src = bass.AP(same_d, ((s * SLOTS + i0) * WIDE + i0 + 1) * GROUPS,
                                      [[(WIDE + 1) * GROUPS, ROWS_I], [GROUPS, DELTAS], [1, GROUPS]])
                        sp.dma_start(inter[dst], src).then_inc(pairs_loaded, 16)
                        src = bass.AP(cross_d, ((s * WIDE + i0 + 1) * NF + i0) * GROUPS,
                                      [[(NF + 1) * GROUPS, ROWS_I], [NF * GROUPS, DELTAS], [1, GROUPS]])
                        sp.dma_start(inter_cross[dst], src).then_inc(pairs_loaded, 16)

            def store_y(t, par):
                wait(sp, y_ready, t + 1, steps_reached)
                sp.dma_start(out_t[t], y[:, par, :]).then_inc(y_stored, 16)

            load_ids(0, 0)
            sp.dma_start(identity[:], eye).then_inc(consts_loaded, 16)
            for n in range(STAGES):
                load_weight(n)
            load_ids(1, 1)
            sp.dma_start(b1_sb[:], b1_t).then_inc(consts_loaded, 16)
            sp.dma_start(b2_rows[:], b2.partition_broadcast(P)).then_inc(consts_loaded, 16)
            sp.dma_start(w3_rows[:], w3.partition_broadcast(P)).then_inc(consts_loaded, 16)
            for n in range(STAGES, len(STAGED)):
                load_weight(n)

            def tile(t, par, more=True):
                if more:
                    wait(sp, quad_transposed, (t + 1) * NQ, steps_reached)
                    load_ids(t + 2, par)
                pairs_round_trip(t)

            sp.wait_ge(zeroed, 1)
            tile(0, 0)
            with sp.Fori(0, TILES // 2 - 2) as i:
                for k in range(2):
                    tile(2 * i + 1 + k, (1 + k) % 2)
                    store_y(2 * i + k, k % 2)
            for t in range(TILES - 3, TILES):
                tile(t, t % 2, more=t + 2 < TILES)
                store_y(t - 1, (t - 1) % 2)
            store_y(TILES - 1, (TILES - 1) % 2)
            sp.wait_ge(y_stored, TILES * 16)

        @block.gpsimd
        def _(pool):
            def gathers(t, par, loads):
                wait(pool, ids_loaded[par], loads * 16, quads_free)
                for q, quad in enumerate(QUADS):
                    wait(pool, quad_transposed, (t - 1) * NQ + q + 1, quads_free)
                    for f in quad:
                        pool.indirect_dma_start(
                            gathered[:, f, :], None, tables[f],
                            bass.IndirectOffsetOnAxis(ap=idx[:, par, f:f + 1], axis=0),
                        ).then_inc(quad_gathered[q], 16)

            gathers(0, 0, 1)
            gathers(1, 1, 1)
            with pool.Fori(1, TILES // 2) as i:
                for k in range(2):
                    gathers(2 * i + k, k, i + 1)

        @block.scalar
        def _(act):
            def weight_high(n):
                kind, c, rows = STAGED[n]
                slot = n % STAGES
                act.wait_ge(w_loaded[slot], (n // STAGES + 1) * 16)
                if kind == "w1":
                    dst, src = w1_high[0:rows, c, :], w_stage[0:rows, slot, :]
                else:
                    dst = w2_high[:, c:c + 2, :].rearrange("p c n -> p (c n)")
                    src = w_stage[:, slot, :]
                nc.scalar.activation(dst, src, ACT.Copy).then_inc(w_high_done, 1)

            def quad_high(t, q, par):
                f0, n = QUADS[q][0], len(QUADS[q])
                if q == 0:
                    wait(act, prod_batch_done, t * NB)
                act.wait_ge(quad_transposed, t * NQ + q + 1)
                nc.scalar.activation(emb[:, :, 0, f0:f0 + n].rearrange("p b f -> p f b"),
                                     p_quad[(par * NQ + q) % 2][:, 0:n, :], ACT.Copy).then_inc(quad_high_done, 1)

            def low_rows(t, b):
                act.wait_ge(prod_batch_done, t * NB + b + 1)
                if b == 0:
                    wait(act, prod_stored, t * (STORES * 16))
                for s in range(2):
                    src = p_prod[b % 2][64 * s + SLOTS:64 * s + SLOTS + NF, 0:2 * COLS * BATCH_G]
                    src = src.rearrange("p (g s c) -> p s g c", s=2, c=COLS)[:, s, :, 0:NF]
                    lo = 64 + SLOTS * s
                    dst = prod[lo:lo + NF, :, b * BATCH_G:(b + 1) * BATCH_G].rearrange("p c g -> p g c")
                    last = nc.scalar.activation(dst, src, ACT.Copy)
                    last.then_inc(low_rows_copied, 1)

            def inter_to_high(t):
                act.wait_ge(inter_summed, t + 1)
                wait(act, hid1_done, t)
                nc.scalar.activation(by_half(inter_high[:]), by_group(inter[:]), ACT.Copy).then_inc(inter_high_done, 1)

            def relu1(t):
                act.wait_ge(hid1_transposed, t + 1)
                wait(act, hid1_low_done, t)
                for c in range(C1):
                    nc.scalar.activation(hid1_relu[:, c, :], p_hid1_t[:, c, :], ACT.Relu,
                                         bias=b1_sb[:, c:c + 1]).then_inc(hid1_relu_done, 1)
                act.wait_ge(hid1_relu_done, (t + 1) * C1)
                wait(act, hid2_done, t)
                nc.scalar.activation(hid1_high[:], hid1_relu[:], ACT.Copy).then_inc(hid1_high_done, 1)

            def tile(t, par, first=False):
                for q in range(NQ):
                    if first:
                        for n in range(4 * q, min(4 * q + 4, NF)):
                            weight_high(n)
                    quad_high(t, q, par)
                    if q == 2 and not first:
                        inter_to_high(t - 1)
                    if q == 4 and not first:
                        relu1(t - 1)
                if first:
                    for n in range(NF, len(STAGED)):
                        weight_high(n)
                for b in range(NB):
                    low_rows(t, b)

            act.wait_ge(consts_loaded, CONSTS * 16)
            act.wait_ge(zeroed, 1)
            tile(0, 0, first=True)
            tile(1, 1)
            tile(2, 0)
            with act.Fori(0, TILES // 2 - 2) as i:
                for k in range(2):
                    tile(2 * i + 3 + k, (1 + k) % 2)
            tile(TILES - 1, (TILES - 1) % 2)
            inter_to_high(TILES - 1)
            relu1(TILES - 1)

        @block.vector
        def _(dve):
            def weight_low(n):
                kind, c, rows = STAGED[n]
                slot = n % STAGES
                dve.wait_ge(w_high_done, n + 1)
                if kind == "w1":
                    dst, src = w1_low[0:rows, c, :], w_stage[0:rows, slot, :]
                    high = w1_high[:].bitcast(F32)[0:rows, c, :]
                else:
                    dst = w2_low[:, c:c + 2, :].rearrange("p c n -> p (c n)")
                    src = w_stage[:, slot, :]
                    high = w2_high[:].bitcast(F32)[:, c:c + 2, :].rearrange("p c n -> p (c n)")
                nc.vector.tensor_tensor(dst, src, high, ALU.subtract).then_inc(w_low_done, 1)

            def quad_low(t, q, par):
                f0, n = QUADS[q][0], len(QUADS[q])
                dve.wait_ge(quad_high_done, t * NQ + q + 1)
                nc.vector.tensor_tensor(emb[:, :, 1, f0:f0 + n].rearrange("p b f -> p f b"),
                                        p_quad[(par * NQ + q) % 2][:, 0:n, :],
                                        emb_f32[:, :, 0, f0:f0 + n].rearrange("p b f -> p f b"),
                                        ALU.subtract).then_inc(quad_low_done, 1)

            def product_sums(t, b):
                dve.wait_ge(low_rows_copied, 2 * (t * NB + b + 1))
                for s in range(2):
                    src = p_prod[b % 2][64 * s:64 * s + NF, 0:2 * COLS * BATCH_G]
                    src = src.rearrange("p (g s c) -> p s g c", s=2, c=COLS)[:, s, :, 0:NF]
                    g = slice(b * BATCH_G, (b + 1) * BATCH_G)
                    low = prod[64 + SLOTS * s:64 + SLOTS * s + NF, :, g].rearrange("p c g -> p g c")
                    dst = prod[SLOTS * s:SLOTS * s + NF, :, g].rearrange("p c g -> p g c")
                    last = nc.vector.tensor_tensor(dst, src, low, ALU.add)
                last.then_inc(prod_summed, 1)

            def inter_sum(t):
                dve.wait_ge(pairs_loaded, (t + 1) * (PAIR_DMAS * 16))
                nc.vector.tensor_tensor(inter[:], inter[:], inter_cross[:], ALU.add).then_inc(inter_summed, 1)

            def inter_to_low(t):
                dve.wait_ge(inter_high_done, t + 1)
                nc.vector.tensor_tensor(by_half(inter_low[:]), by_group(inter[:]), by_half(inter_high_f32),
                                        ALU.subtract).then_inc(inter_low_done, 1)

            def copy_hid1(t, par):
                dve.wait_ge(hid1_done, t + 1)
                wait(dve, hid1_transposed, t)
                nc.vector.tensor_copy(hid1[:], p_hid1[par][:]).then_inc(hid1_copied, 1)

            def hid1_to_low(t):
                dve.wait_ge(hid1_high_done, t + 1)
                nc.vector.tensor_tensor(hid1_low[:], hid1_relu[:], hid1_high_f32, ALU.subtract).then_inc(hid1_low_done, 1)

            def layer3(t, par):
                dve.wait_ge(hid2_done, t + 1)
                nc.vector.tensor_tensor(hid2[:], p_hid2[:, 0:HID2], b2_rows[:], ALU.add).then_inc(hid2_step, 1)
                dve.wait_ge(hid2_step, 2 * t + 1)
                nc.vector.tensor_scalar(hid2[:], hid2[:], 0.0, None, ALU.max).then_inc(hid2_step, 1)
                dve.wait_ge(hid2_step, 2 * t + 2)
                wait(dve, y_stored, (t - 1) * 16)
                nc.vector.tensor_tensor_reduce(out=hid2[:], in0=hid2[:], in1=w3_rows[:], scale=1.0, scalar=0.0,
                                               op0=ALU.mult, op1=ALU.add, accum_out=y[:, par, :]).then_inc(y_ready, 1)

            def tile(t, par, first=False):
                for q in range(NQ):
                    if first:
                        for n in range(4 * q, min(4 * q + 4, NF)):
                            weight_low(n)
                    quad_low(t, q, par)
                    if first:
                        continue
                    if q == 1:
                        inter_sum(t - 1)
                    if q == 2:
                        inter_to_low(t - 1)
                    if q == 3:
                        copy_hid1(t - 1, (par + 1) % 2)
                    if q == 4:
                        hid1_to_low(t - 1)
                if first:
                    for n in range(NF, len(STAGED)):
                        weight_low(n)
                for b in range(NB):
                    product_sums(t, b)
                if not first:
                    layer3(t - 1, (par + 1) % 2)

            nc.vector.memset(emb_f32[:, :, :, NF:SLOTS], 0.0)
            nc.vector.memset(prod[:], 0.0)
            nc.vector.memset(inter[:], 0.0)
            nc.vector.memset(inter_cross[:], 0.0).then_inc(zeroed, 1)
            dve.wait_ge(zeroed, 1)
            dve.wait_ge(consts_loaded, CONSTS * 16)
            tile(0, 0, first=True)
            tile(1, 1)
            tile(2, 0)
            with dve.Fori(0, TILES // 2 - 2) as i:
                for k in range(2):
                    tile(2 * i + 3 + k, (1 + k) % 2)
            tile(TILES - 1, (TILES - 1) % 2)
            last = TILES - 1
            inter_sum(last)
            inter_to_low(last)
            copy_hid1(last, last % 2)
            hid1_to_low(last)
            layer3(last, last % 2)

        @block.tensor
        def _(pe):
            def transpose_quad(t, q, par):
                n = len(QUADS[q])
                pe.wait_ge(quad_gathered[q], (t + 1) * (n * 16))
                wait(pe, quad_low_done, t * NQ + q - 1)
                for k, f in enumerate(QUADS[q]):
                    last = nc.tensor.transpose(p_quad[(par * NQ + q) % 2][:, k, :], gathered[:, f, :], identity[:])
                last.then_inc(quad_transposed, 1)

            def three_passes(dst, high, low, w_high, w_low, start, stop):
                nc.tensor.matmul(dst, high, w_high, start=start, stop=False)
                nc.tensor.matmul(dst, high, w_low, start=False, stop=False)
                return nc.tensor.matmul(dst, low, w_high, start=False, stop=stop)

            def layer1_feature(f, par, first):
                if first:
                    pe.wait_ge(w_low_done, f + 1)
                three_passes(p_hid1[par][:], emb[:, :, 0, f], emb[:, :, 1, f],
                             w1_high[:, f, :], w1_low[:, f, :], f == 0, False)

            def layer1_quad(t, q, par, first):
                if q == 0:
                    wait(pe, hid1_copied, t - 1)
                pe.wait_ge(quad_low_done, t * NQ + q + 1)
                for f in QUADS[q]:
                    layer1_feature(f, par, first)

            def layer1_pairs(t, par):
                pe.wait_ge(inter_low_done, t + 1)
                for c in range(3):
                    k = K_PAIR[c]
                    last = three_passes(p_hid1[par][:], inter_high[0:k, c, :], inter_low[0:k, c, :],
                                        w1_high[0:k, NF + c, :], w1_low[0:k, NF + c, :], False, c == 2)
                last.then_inc(hid1_done, 1)

            def transpose_hid1(t):
                pe.wait_ge(hid1_copied, t + 1)
                wait(pe, hid1_relu_done, t * C1)
                for c in range(C1):
                    last = nc.tensor.transpose(p_hid1_t[:, c, :], hid1[:, c * P:(c + 1) * P], identity[:])
                last.then_inc(hid1_transposed, 1)

            def layer2(t):
                pe.wait_ge(hid1_low_done, t + 1)
                wait(pe, y_ready, t)
                for c in range(C1):
                    last = three_passes(p_hid2[:, 0:HID2], hid1_high[:, c, :], hid1_low[:, c, :],
                                        w2_high[:, c, :], w2_low[:, c, :], c == 0, c == C1 - 1)
                last.then_inc(hid2_done, 1)

            def product_batch(t, b):
                wait(pe, prod_summed, t * NB + b - 1)
                for k in range(BATCH_G):
                    g = b * BATCH_G + k
                    both = emb[:, 2 * g:2 * g + 2, :, :]
                    last = nc.tensor.matmul(p_prod[b % 2][:, 2 * COLS * k:2 * COLS * (k + 1)],
                                            both.rearrange("p s h f -> p s (h f)"),
                                            both[:, :, 0, 0:COLS], start=True, stop=True)
                last.then_inc(prod_batch_done, 1)

            def tile(t, par, first=False):
                other = (par + 1) % 2
                for q in range(NQ):
                    transpose_quad(t, q, par)
                    if 1 <= q < NQ - 1:
                        layer1_quad(t, q - 1, par, first)
                    if first:
                        continue
                    if q == 3:
                        layer1_pairs(t - 1, other)
                    if q == 4:
                        transpose_hid1(t - 1)
                    if q == 6:
                        layer2(t - 1)
                pe.wait_ge(quad_low_done, t * NQ + NQ - 1)
                left = QUADS[NQ - 2] + QUADS[NQ - 1]
                for f in left[:2]:
                    layer1_feature(f, par, first)
                left = left[2:]
                pe.wait_ge(quad_low_done, (t + 1) * NQ)
                for b in range(NB):
                    if b >= 2 and left:
                        layer1_feature(left.pop(0), par, first)
                    product_batch(t, b)
                assert not left

            pe.wait_ge(consts_loaded, CONSTS * 16)
            tile(0, 0, first=True)
            pe.wait_ge(w_low_done, len(STAGED))
            tile(1, 1)
            tile(2, 0)
            with pe.Fori(0, TILES // 2 - 2) as i:
                for k in range(2):
                    tile(2 * i + 3 + k, (1 + k) % 2)
            tile(TILES - 1, (TILES - 1) % 2)
            last = TILES - 1
            layer1_pairs(last, last % 2)
            transpose_hid1(last)
            layer2(last)


N_TABLES = 27


def kernel(**inputs):
    import numpy as np
    import concourse.bacc as bacc
    from concourse.bass_utils import run_bass_kernel_spmd

    nc = bacc.Bacc("TRN2", target_bir_lowering=False, num_devices=1)
    w1 = np.asarray(inputs["W_top1"])
    dense_ctx = np.asarray(inputs["dense_ctx"])
    pair_rows, _ = pair_layout(N_TABLES, dense_ctx.shape[1])
    pair_rows = np.array([r for chunk in pair_rows for r in chunk])
    arrays = {
        "ids": np.asarray(inputs["ids"]),
        "ctx_t": np.ascontiguousarray(
            dense_ctx.reshape(-1, P // 2, 2, dense_ctx.shape[1]).transpose(3, 0, 2, 1)
        ).reshape(dense_ctx.shape[1], -1),
        "w_dense": np.ascontiguousarray(w1[:N_TABLES * P]),
        "w_pairs": np.ascontiguousarray(w1[pair_rows]),
        "b1_t": np.ascontiguousarray(np.asarray(inputs["b_top1"]).reshape(-1, P).T),
        "w2": np.asarray(inputs["W_top2"]),
        "b2": np.asarray(inputs["b_top2"]),
        "w3": np.asarray(inputs["W_top3"]).reshape(-1),
        "eye": np.eye(P, dtype=np.float32),
    }
    for f in range(N_TABLES):
        arrays[f"tbl_{f}"] = np.asarray(inputs[f"tbl_{f}"])
    arrays = {k + "_dram": np.ascontiguousarray(v) for k, v in arrays.items()}
    aps = {k[:-5]: nc.dram_tensor(k, v.shape, mybir.dt.from_np(v.dtype), kind="ExternalInput").ap()
           for k, v in arrays.items()}
    out = nc.dram_tensor("out_dram", (dense_ctx.shape[0], 1), F32, kind="ExternalOutput").ap()
    dlrm_tower(nc, aps["ids"], [aps[f"tbl_{f}"] for f in range(N_TABLES)], aps["ctx_t"], aps["w_dense"],
               aps["w_pairs"], aps["b1_t"], aps["w2"], aps["b2"], aps["w3"], aps["eye"], out)
    r = run_bass_kernel_spmd(nc, [arrays], core_ids=[0])
    return r.results[0]["out_dram"]
```

```python
from contextlib import ExitStack

import concourse.bass as bass
from concourse import mybir

F32 = mybir.dt.float32
F32R = mybir.dt.float32r
I32 = mybir.dt.int32
ACT = mybir.ActivationFunctionType
ALU = mybir.AluOpType

P = 128


def pair_layout(features, ctx_rows):
    deltas = (features - 1) // 2
    per_chunk = features // 3
    first_pair = features * P
    first_ctx = first_pair + features * (features - 1) // 2
    room = P - per_chunk * deltas
    ctx_in_chunk = [min(room, ctx_rows), ctx_rows - min(room, ctx_rows), 0]
    rows, taken = [], 0
    for c in range(3):
        rows.append([first_ctx + taken + k for k in range(ctx_in_chunk[c])])
        taken += ctx_in_chunk[c]
        for i in range(c * per_chunk, (c + 1) * per_chunk):
            for delta in range(1, deltas + 1):
                a, b = sorted((i, (i + delta) % features))
                rows[c].append(first_pair + a * features - a * (a + 1) // 2 + b - a - 1)
    return rows, ctx_in_chunk


def dlrm_tower(nc, ids, tables, ctx_t, w_dense, w_pairs, b1_t, w2, b2, w3, eye, out):
    B, NF = ids.shape
    D = tables[0].shape[1]
    HID1 = w_dense.shape[1]
    HID2 = w2.shape[1]
    TILES = B // P
    CTX = ctx_t.shape[0]
    assert D == P and B % P == 0 and TILES % 2 == 0 and NF % 3 == 0 and NF % 2 == 1
    assert HID1 == 512 and HID2 <= 512 and HID1 % P == 0

    pair_rows, ctx_in_chunk = pair_layout(NF, CTX)
    DELTAS = (NF - 1) // 2
    ROWS_I = NF // 3
    K_PAIR = [len(r) for r in pair_rows]
    CHUNKS = NF + 3
    C1 = HID1 // P

    QUADS = [list(range(f, min(f + 4, NF))) for f in range(0, NF, 4)]
    NQ = len(QUADS)
    QUARTERS = 4
    SLOTS = P // QUARTERS
    GROUPS = P // QUARTERS
    NB = 2
    BATCH_G = GROUPS // NB
    WRAP = DELTAS
    WIDE = NF + WRAP
    STAGES = 4

    ids_t = ids.rearrange("(t p) f -> t p f", p=P)
    out_t = out.rearrange("(t p) o -> t p o", p=P)

    pairs_d = nc.dram_tensor("pairs_dram", [QUARTERS, SLOTS, WIDE, GROUPS], F32, kind="Internal")
    pairs_rows = pairs_d.ap().rearrange("s r c g -> (s r) c g")

    with ExitStack() as ctx:
        def sb(name, shape, dt=F32):
            return ctx.enter_context(nc.sbuf_tensor(name, shape, dt))

        def pb(name, shape):
            return ctx.enter_context(nc.psum_tensor(name, shape, F32))

        def sem(name):
            return ctx.enter_context(nc.semaphore(name))

        w1_high = sb("w1_high", [P, CHUNKS, HID1], F32R)
        w1_low = sb("w1_low", [P, CHUNKS, HID1], F32R)
        w2_high = sb("w2_high", [P, C1, HID2], F32R)
        w2_low = sb("w2_low", [P, C1, HID2], F32R)
        b1_sb = sb("b1_sb", [P, C1])
        b2_rows = sb("b2_rows", [P, HID2])
        w3_rows = sb("w3_rows", [P, HID2])
        identity = sb("identity", [P, P])
        w_stage = sb("w_stage", [P, STAGES, HID1])
        idx = sb("idx", [P, 2, NF], I32)
        gathered = sb("gathered", [P, NF, D])
        emb = sb("emb", [P, P, NF])
        emb_high = sb("emb_high", [P, NF, P], F32R)
        emb_low = sb("emb_low", [P, NF, P], F32R)
        emb_high_f32 = emb_high[:].bitcast(F32)
        prod = sb("prod", [P, NF, GROUPS])
        inter = sb("inter", [P, 3, P])
        inter_high = sb("inter_high", [P, 3, P], F32R)
        inter_low = sb("inter_low", [P, 3, P], F32R)
        inter_high_f32 = inter_high[:].bitcast(F32)
        hid1 = sb("hid1", [P, HID1])
        hid1_t = hid1[:].rearrange("p (c b) -> p c b", c=C1)
        hid1_high = sb("hid1_high", [P, C1, P], F32R)
        hid1_low = sb("hid1_low", [P, C1, P], F32R)
        hid1_high_f32 = hid1_high[:].bitcast(F32)
        hid2 = sb("hid2", [P, HID2])
        y = sb("y", [P, 2, 1])

        p_hid1 = [pb(f"p_hid1_{k}", [P, HID1]) for k in range(2)]
        p_quad = [pb(f"p_quad_{k}", [P, 4, P]) for k in range(2)]
        p_prod = [pb(f"p_prod_{k}", [P, 512]) for k in range(2)]
        p_hid1_t = pb("p_hid1_t", [P, C1, P])
        p_hid2 = pb("p_hid2", [P, 512])

        consts_loaded = sem("consts_loaded")
        w_loaded = [sem(f"w_loaded_{k}") for k in range(STAGES)]
        ids_loaded = [sem(f"ids_loaded_{k}") for k in range(2)]
        quad_gathered = [sem(f"quad_gathered_{q}") for q in range(NQ)]
        prod_stored = sem("prod_stored")
        pairs_loaded = sem("pairs_loaded")
        last_pairs_loaded = sem("last_pairs_loaded")
        y_stored = sem("y_stored")
        quads_free = sem("quads_free")
        steps_reached = sem("steps_reached")
        quad_transposed = sem("quad_transposed")
        quad_used = sem("quad_used")
        prod_bank_done = sem("prod_bank_done")
        hid1_done = sem("hid1_done")
        hid1_transposed = sem("hid1_transposed")
        hid2_done = sem("hid2_done")
        w_high_done = sem("w_high_done")
        quad_copied = sem("quad_copied")
        prod_copied_act = sem("prod_copied_act")
        inter_high_done = sem("inter_high_done")
        hid1_relu_done = sem("hid1_relu_done")
        hid1_high_done = sem("hid1_high_done")
        zeroed = sem("zeroed")
        w_low_done = sem("w_low_done")
        quad_low_done = sem("quad_low_done")
        prod_copied_dve = sem("prod_copied_dve")
        inter_low_done = sem("inter_low_done")
        hid1_copied = sem("hid1_copied")
        hid1_low_done = sem("hid1_low_done")
        hid2_step = sem("hid2_step")
        y_ready = sem("y_ready")

        def wait(eng, s, value, carrier=None):
            if not isinstance(value, int) or value > 0:
                eng.wait_ge(s, value)
                if carrier is not None and not isinstance(value, int):
                    eng.sem_inc(carrier, 1)

        W1_CHUNKS = [("w1", c, P if c < NF else K_PAIR[c - NF]) for c in range(CHUNKS)]
        W2_PAIRS = [("w2", c, P) for c in range(0, C1, 2)]
        STAGED = W1_CHUNKS + W2_PAIRS
        pair_base = [sum(K_PAIR[:c]) for c in range(3)]
        PAIR_DMAS = 3 * QUARTERS + sum(1 for n in ctx_in_chunk if n)
        STORES = 2
        ALL_PARTS = [(c, s) for c in range(3) for s in range(QUARTERS)]
        LATE = 5
        CONSTS = 4

        def product_copy(b):
            src = p_prod[b][:, 0:BATCH_G * NF].rearrange("p (g c) -> p g c", c=NF)
            return prod[:, :, b * BATCH_G:(b + 1) * BATCH_G].rearrange("p c g -> p g c"), src

        def load_pairs(eng, parts, loaded):
            for c, s in parts:
                lo, i0 = ctx_in_chunk[c], c * ROWS_I
                src = bass.AP(pairs_d, ((s * SLOTS + i0) * WIDE + i0 + 1) * GROUPS,
                              [[(WIDE + 1) * GROUPS, ROWS_I], [GROUPS, DELTAS], [1, GROUPS]])
                eng.dma_start(inter[lo:lo + ROWS_I * DELTAS, c, s * GROUPS:(s + 1) * GROUPS],
                              src).then_inc(loaded, 16)

        block = ctx.enter_context(nc.Block())

        @block.sync
        def _(sp):
            def load_ids(t, par):
                sp.dma_start(idx[:, par, :], ids_t[t]).then_inc(ids_loaded[par], 16)

            def load_weight(n):
                kind, c, rows = STAGED[n]
                wait(sp, w_low_done, n - STAGES + 1, steps_reached)
                slot = n % STAGES
                if kind == "w1" and c < NF:
                    src, dst = w_dense[c * P:(c + 1) * P, :], w_stage[:, slot, :]
                elif kind == "w1":
                    src = w_pairs[pair_base[c - NF]:pair_base[c - NF] + rows, :]
                    dst = w_stage[0:rows, slot, :]
                else:
                    src = w2.rearrange("(c p) n -> p c n", p=P)[:, c:c + 2, :]
                    dst = w_stage[:, slot, :].rearrange("p (c n) -> p c n", c=2)
                sp.dma_start(dst, src).then_inc(w_loaded[slot], 16)

            def pairs_round_trip(t, parts):
                wait(sp, prod_copied_act, t + 1, steps_reached)
                wait(sp, prod_copied_dve, t + 1, steps_reached)
                wait(sp, pairs_loaded, t * (PAIR_DMAS * 16), steps_reached)
                sp.dma_start(pairs_rows[:, 0:NF, :], prod[:]).then_inc(prod_stored, 16)
                sp.dma_start(pairs_rows[:, NF:WIDE, :], prod[:, 0:WRAP, :]).then_inc(prod_stored, 16)
                wait(sp, inter_low_done, t, steps_reached)
                k = 0
                for c in range(3):
                    n = ctx_in_chunk[c]
                    if n:
                        sp.dma_start(inter[0:n, c, :],
                                     ctx_t[k:k + n, bass.ds(t * P, P)]).then_inc(pairs_loaded, 16)
                        k += n
                wait(sp, prod_stored, (t + 1) * (STORES * 16), steps_reached)
                load_pairs(sp, parts, pairs_loaded)

            def store_y(t, par):
                wait(sp, y_ready, t + 1, steps_reached)
                sp.dma_start(out_t[t], y[:, par, :]).then_inc(y_stored, 16)

            load_ids(0, 0)
            sp.dma_start(identity[:], eye).then_inc(consts_loaded, 16)
            for n in range(STAGES):
                load_weight(n)
            load_ids(1, 1)
            sp.dma_start(b1_sb[:], b1_t).then_inc(consts_loaded, 16)
            sp.dma_start(b2_rows[:], b2.partition_broadcast(P)).then_inc(consts_loaded, 16)
            sp.dma_start(w3_rows[:], w3.partition_broadcast(P)).then_inc(consts_loaded, 16)
            for n in range(STAGES, len(STAGED)):
                load_weight(n)

            def tile(t, par, more=True, parts=ALL_PARTS):
                if more:
                    wait(sp, quad_transposed, (t + 1) * NQ, steps_reached)
                    load_ids(t + 2, par)
                pairs_round_trip(t, parts)

            sp.wait_ge(zeroed, 1)
            tile(0, 0)
            with sp.Fori(0, TILES // 2 - 2) as i:
                for k in range(2):
                    tile(2 * i + 1 + k, (1 + k) % 2)
                    store_y(2 * i + k, k % 2)
            for t in range(TILES - 3, TILES - 1):
                tile(t, t % 2, more=t + 2 < TILES)
                store_y(t - 1, (t - 1) % 2)
            tile(TILES - 1, (TILES - 1) % 2, more=False, parts=ALL_PARTS[LATE:])
            store_y(TILES - 2, (TILES - 2) % 2)
            store_y(TILES - 1, (TILES - 1) % 2)
            sp.wait_ge(y_stored, TILES * 16)

        @block.gpsimd
        def _(pool):
            def gathers(t, par, loads):
                wait(pool, ids_loaded[par], loads * 16, quads_free)
                for q, quad in enumerate(QUADS):
                    wait(pool, quad_transposed, (t - 1) * NQ + q + 1, quads_free)
                    for f in quad:
                        pool.indirect_dma_start(
                            gathered[:, f, :], None, tables[f],
                            bass.IndirectOffsetOnAxis(ap=idx[:, par, f:f + 1], axis=0),
                        ).then_inc(quad_gathered[q], 16)

            gathers(0, 0, 1)
            gathers(1, 1, 1)
            with pool.Fori(1, TILES // 2) as i:
                for k in range(2):
                    gathers(2 * i + k, k, i + 1)
            pool.wait_ge(inter_low_done, TILES - 1)
            pool.wait_ge(prod_stored, TILES * (STORES * 16))
            load_pairs(pool, ALL_PARTS[:LATE], last_pairs_loaded)

        @block.scalar
        def _(act):
            def weight_high(n):
                kind, c, rows = STAGED[n]
                slot = n % STAGES
                act.wait_ge(w_loaded[slot], (n // STAGES + 1) * 16)
                if kind == "w1":
                    dst, src = w1_high[0:rows, c, :], w_stage[0:rows, slot, :]
                else:
                    dst = w2_high[:, c:c + 2, :].rearrange("p c n -> p (c n)")
                    src = w_stage[:, slot, :]
                nc.scalar.activation(dst, src, ACT.Copy).then_inc(w_high_done, 1)

            def quad_copies(t, q, par):
                f0, n = QUADS[q][0], len(QUADS[q])
                bank = p_quad[(par * NQ + q) % 2][:, 0:n, :]
                act.wait_ge(quad_transposed, t * NQ + q + 1)
                wait(act, quad_used, (t - 1) * NQ + q + 1)
                nc.scalar.activation(emb_high[:, f0:f0 + n, :], bank, ACT.Copy)
                if q == 0:
                    wait(act, prod_bank_done, t * NB)
                nc.scalar.activation(emb[:, :, f0:f0 + n].rearrange("p b f -> p f b"), bank,
                                     ACT.Copy).then_inc(quad_copied, 1)

            def copy_products(t):
                act.wait_ge(prod_bank_done, t * NB + 1)
                wait(act, prod_stored, t * (STORES * 16))
                nc.scalar.activation(*product_copy(0), ACT.Copy).then_inc(prod_copied_act, 1)

            def inter_to_high(t, by_gpsimd=0):
                act.wait_ge(pairs_loaded, (t + 1) * (PAIR_DMAS * 16) - by_gpsimd * 16)
                wait(act, last_pairs_loaded, by_gpsimd * 16)
                wait(act, hid1_done, t)
                nc.scalar.activation(inter_high[:], inter[:], ACT.Copy).then_inc(inter_high_done, 1)

            def relu1(t):
                act.wait_ge(hid1_transposed, t + 1)
                for c in range(C1):
                    nc.scalar.activation(hid1_t[:, c, :], p_hid1_t[:, c, :], ACT.Relu,
                                         bias=b1_sb[:, c:c + 1]).then_inc(hid1_relu_done, 1)
                act.wait_ge(hid1_relu_done, (t + 1) * C1)
                wait(act, hid2_done, t)
                nc.scalar.activation(hid1_high[:], hid1_t, ACT.Copy).then_inc(hid1_high_done, 1)

            def tile(t, par, first=False):
                for q in range(NQ):
                    if first:
                        for n in range(4 * q, min(4 * q + 4, NF)):
                            weight_high(n)
                    quad_copies(t, q, par)
                    if q == 4 and not first:
                        inter_to_high(t - 1)
                if first:
                    for n in range(NF, len(STAGED)):
                        weight_high(n)
                copy_products(t)
                if not first:
                    relu1(t - 1)

            act.wait_ge(consts_loaded, CONSTS * 16)
            act.wait_ge(zeroed, 1)
            tile(0, 0, first=True)
            tile(1, 1)
            tile(2, 0)
            with act.Fori(0, TILES // 2 - 2) as i:
                for k in range(2):
                    tile(2 * i + 3 + k, (1 + k) % 2)
            tile(TILES - 1, (TILES - 1) % 2)
            inter_to_high(TILES - 1, by_gpsimd=LATE)
            relu1(TILES - 1)

        @block.vector
        def _(dve):
            def weight_low(n):
                kind, c, rows = STAGED[n]
                slot = n % STAGES
                dve.wait_ge(w_high_done, n + 1)
                if kind == "w1":
                    dst, src = w1_low[0:rows, c, :], w_stage[0:rows, slot, :]
                    high = w1_high[:].bitcast(F32)[0:rows, c, :]
                else:
                    dst = w2_low[:, c:c + 2, :].rearrange("p c n -> p (c n)")
                    src = w_stage[:, slot, :]
                    high = w2_high[:].bitcast(F32)[:, c:c + 2, :].rearrange("p c n -> p (c n)")
                nc.vector.tensor_tensor(dst, src, high, ALU.subtract).then_inc(w_low_done, 1)

            def quad_low(t, q, par):
                f0, n = QUADS[q][0], len(QUADS[q])
                dve.wait_ge(quad_copied, t * NQ + q + 1)
                wait(dve, quad_used, (t - 1) * NQ + q + 1)
                nc.vector.tensor_tensor(emb_low[:, f0:f0 + n, :], p_quad[(par * NQ + q) % 2][:, 0:n, :],
                                        emb_high_f32[:, f0:f0 + n, :], ALU.subtract).then_inc(quad_low_done, 1)

            def copy_products(t):
                dve.wait_ge(prod_bank_done, t * NB + 2)
                wait(dve, prod_stored, t * (STORES * 16))
                nc.vector.tensor_copy(*product_copy(1)).then_inc(prod_copied_dve, 1)

            def inter_to_low(t):
                dve.wait_ge(inter_high_done, t + 1)
                nc.vector.tensor_tensor(inter_low[:], inter[:], inter_high_f32, ALU.subtract).then_inc(inter_low_done, 1)

            def copy_hid1(t, par):
                dve.wait_ge(hid1_done, t + 1)
                wait(dve, hid1_low_done, t)
                nc.vector.tensor_copy(hid1[:], p_hid1[par][:]).then_inc(hid1_copied, 1)

            def hid1_to_low(t):
                dve.wait_ge(hid1_high_done, t + 1)
                nc.vector.tensor_tensor(hid1_low[:], hid1_t, hid1_high_f32, ALU.subtract).then_inc(hid1_low_done, 1)

            def layer3(t, par):
                dve.wait_ge(hid2_done, t + 1)
                nc.vector.tensor_tensor(hid2[:], p_hid2[:, 0:HID2], b2_rows[:], ALU.add).then_inc(hid2_step, 1)
                dve.wait_ge(hid2_step, 2 * t + 1)
                nc.vector.tensor_scalar(hid2[:], hid2[:], 0.0, None, ALU.max).then_inc(hid2_step, 1)
                dve.wait_ge(hid2_step, 2 * t + 2)
                wait(dve, y_stored, (t - 1) * 16)
                nc.vector.tensor_tensor_reduce(out=hid2[:], in0=hid2[:], in1=w3_rows[:], scale=1.0, scalar=0.0,
                                               op0=ALU.mult, op1=ALU.add, accum_out=y[:, par, :]).then_inc(y_ready, 1)

            def tile(t, par, first=False, second=False, final=False):
                for q in range(NQ):
                    if first:
                        for n in range(4 * q, min(4 * q + 4, NF)):
                            weight_low(n)
                    quad_low(t, q, par)
                    if first:
                        continue
                    if q == 1 and not second:
                        layer3(t - 2, par)
                    if q == 4:
                        inter_to_low(t - 1)
                    if q == 5 and not final:
                        copy_hid1(t - 1, (par + 1) % 2)
                if first:
                    for n in range(NF, len(STAGED)):
                        weight_low(n)
                copy_products(t)
                if final:
                    copy_hid1(t - 1, (par + 1) % 2)
                if not first:
                    hid1_to_low(t - 1)

            for bank in p_prod:
                nc.vector.memset(bank[:], 0.0)
            nc.vector.memset(inter[:], 0.0).then_inc(zeroed, 1)
            dve.wait_ge(zeroed, 1)
            dve.wait_ge(consts_loaded, CONSTS * 16)
            tile(0, 0, first=True)
            tile(1, 1, second=True)
            for t in range(2, 5):
                tile(t, t % 2)
            with dve.Fori(0, TILES // 2 - 3) as i:
                for k in range(2):
                    tile(2 * i + 5 + k, (1 + k) % 2)
            tile(TILES - 1, (TILES - 1) % 2, final=True)
            last = TILES - 1
            layer3(last - 1, (last - 1) % 2)
            inter_to_low(last)
            copy_hid1(last, last % 2)
            hid1_to_low(last)
            layer3(last, last % 2)

        @block.tensor
        def _(pe):
            def transpose_quad(t, q, par):
                n = len(QUADS[q])
                pe.wait_ge(quad_gathered[q], (t + 1) * (n * 16))
                wait(pe, quad_low_done, t * NQ + q - 1)
                for k, f in enumerate(QUADS[q]):
                    last = nc.tensor.transpose(p_quad[(par * NQ + q) % 2][:, k, :], gathered[:, f, :], identity[:])
                last.then_inc(quad_transposed, 1)

            def three_passes(dst, high, low, w_high, w_low, start, stop):
                nc.tensor.matmul(dst, high, w_high, start=start, stop=False)
                nc.tensor.matmul(dst, high, w_low, start=False, stop=False)
                return nc.tensor.matmul(dst, low, w_high, start=False, stop=stop)

            def layer1_feature(f, par, first):
                if first:
                    pe.wait_ge(w_low_done, f + 1)
                return three_passes(p_hid1[par][:], emb_high[:, f, :], emb_low[:, f, :],
                                    w1_high[:, f, :], w1_low[:, f, :], f == 0, False)

            def layer1_quad(t, q, par, first):
                if q == 0:
                    wait(pe, hid1_copied, t - 1)
                pe.wait_ge(quad_low_done, t * NQ + q + 1)
                for f in QUADS[q]:
                    last = layer1_feature(f, par, first)
                last.then_inc(quad_used, 1)

            def layer1_pairs(t, par):
                pe.wait_ge(inter_low_done, t + 1)
                for c in range(3):
                    k = K_PAIR[c]
                    last = three_passes(p_hid1[par][:], inter_high[0:k, c, :], inter_low[0:k, c, :],
                                        w1_high[0:k, NF + c, :], w1_low[0:k, NF + c, :], False, c == 2)
                last.then_inc(hid1_done, 1)

            def transpose_hid1(t):
                pe.wait_ge(hid1_copied, t + 1)
                wait(pe, hid1_relu_done, t * C1)
                for c in range(C1):
                    last = nc.tensor.transpose(p_hid1_t[:, c, :], hid1[:, c * P:(c + 1) * P], identity[:])
                last.then_inc(hid1_transposed, 1)

            def layer2(t):
                pe.wait_ge(hid1_low_done, t + 1)
                wait(pe, y_ready, t)
                for c in range(C1):
                    last = three_passes(p_hid2[:, 0:HID2], hid1_high[:, c, :], hid1_low[:, c, :],
                                        w2_high[:, c, :], w2_low[:, c, :], c == 0, c == C1 - 1)
                last.then_inc(hid2_done, 1)

            def pair_products(t, first):
                pe.wait_ge(quad_copied, (t + 1) * NQ)
                if first:
                    pe.wait_ge(zeroed, 1)
                for b in range(NB):
                    if b == 0:
                        wait(pe, prod_copied_act, t)
                    else:
                        wait(pe, prod_copied_dve, t)
                    for k in range(BATCH_G):
                        for s in range(QUARTERS):
                            x = emb[:, s * GROUPS + b * BATCH_G + k, :]
                            last = nc.tensor.matmul(p_prod[b][s * SLOTS:s * SLOTS + NF, k * NF:(k + 1) * NF],
                                                    x, x, start=True, stop=True)
                    last.then_inc(prod_bank_done, 1)

            def tile(t, par, first=False):
                other = (par + 1) % 2
                for q in range(1, NQ):
                    transpose_quad(t, q, par)
                    layer1_quad(t, q - 1, par, first)
                    if q == 5 and not first:
                        layer1_pairs(t - 1, other)
                pair_products(t, first)
                if not first:
                    transpose_hid1(t - 1)
                transpose_quad(t + 1, 0, other)
                layer1_quad(t, NQ - 1, par, first)
                if not first:
                    layer2(t - 1)

            def last_tile(t, par):
                for q in range(1, 4):
                    transpose_quad(t, q, par)
                    layer1_quad(t, q - 1, par, False)
                transpose_quad(t, 4, par)
                transpose_quad(t, 5, par)
                pe.wait_ge(quad_low_done, t * NQ + 4)
                for f in QUADS[3][:2]:
                    layer1_feature(f, par, False)
                transpose_quad(t, 6, par)
                for f in QUADS[3][2:]:
                    layer1_feature(f, par, False)
                pair_products(t, False)
                layer1_pairs(t - 1, (par + 1) % 2)
                for q in range(4, NQ - 1):
                    layer1_quad(t, q, par, False)
                transpose_hid1(t - 1)
                layer1_quad(t, NQ - 1, par, False)
                layer2(t - 1)

            pe.wait_ge(consts_loaded, CONSTS * 16)
            transpose_quad(0, 0, 0)
            tile(0, 0, first=True)
            pe.wait_ge(w_low_done, len(STAGED))
            tile(1, 1)
            tile(2, 0)
            with pe.Fori(0, TILES // 2 - 2) as i:
                for k in range(2):
                    tile(2 * i + 3 + k, (1 + k) % 2)
            last_tile(TILES - 1, (TILES - 1) % 2)
            last = TILES - 1
            layer1_pairs(last, last % 2)
            transpose_hid1(last)
            layer2(last)


N_TABLES = 27


def kernel(**inputs):
    import numpy as np
    import concourse.bacc as bacc
    from concourse.bass_utils import run_bass_kernel_spmd

    nc = bacc.Bacc("TRN2", target_bir_lowering=False, num_devices=1)
    w1 = np.asarray(inputs["W_top1"])
    dense_ctx = np.asarray(inputs["dense_ctx"])
    pair_rows, _ = pair_layout(N_TABLES, dense_ctx.shape[1])
    pair_rows = np.array([r for chunk in pair_rows for r in chunk])
    arrays = {
        "ids": np.asarray(inputs["ids"]),
        "ctx_t": np.ascontiguousarray(dense_ctx.T),
        "w_dense": np.ascontiguousarray(w1[:N_TABLES * P]),
        "w_pairs": np.ascontiguousarray(w1[pair_rows]),
        "b1_t": np.ascontiguousarray(np.asarray(inputs["b_top1"]).reshape(-1, P).T),
        "w2": np.asarray(inputs["W_top2"]),
        "b2": np.asarray(inputs["b_top2"]),
        "w3": np.asarray(inputs["W_top3"]).reshape(-1),
        "eye": np.eye(P, dtype=np.float32),
    }
    for f in range(N_TABLES):
        arrays[f"tbl_{f}"] = np.asarray(inputs[f"tbl_{f}"])
    arrays = {k + "_dram": np.ascontiguousarray(v) for k, v in arrays.items()}
    aps = {k[:-5]: nc.dram_tensor(k, v.shape, mybir.dt.from_np(v.dtype), kind="ExternalInput").ap()
           for k, v in arrays.items()}
    out = nc.dram_tensor("out_dram", (dense_ctx.shape[0], 1), F32, kind="ExternalOutput").ap()
    dlrm_tower(nc, aps["ids"], [aps[f"tbl_{f}"] for f in range(N_TABLES)], aps["ctx_t"], aps["w_dense"],
               aps["w_pairs"], aps["b1_t"], aps["w2"], aps["b2"], aps["w3"], aps["eye"], out)
    r = run_bass_kernel_spmd(nc, [arrays], core_ids=[0])
    return r.results[0]["out_dram"]
```
